# Optimizing a Trainium2 kernel written in Bass

```python
import numpy as np
import jax
import jax.numpy as jnp

def _softmax(x, axis=-1):
    return jax.nn.softmax(x, axis=axis)

def _gelu(x):
    return jax.nn.gelu(x, approximate=True)

def _silu(x):
    return jax.nn.silu(x)

def _sigmoid(x):
    return jax.nn.sigmoid(x)

def _layernorm(x, axis=-1, eps=1e-05):
    m = jnp.mean(x, axis=axis, keepdims=True)
    v = jnp.var(x, axis=axis, keepdims=True)
    return (x - m) / jnp.sqrt(v + eps)

def _scatter_add(tgt, idx, src, axis=0):
    return tgt.at[idx].add(src)

def _segment_sum(src, seg, n):
    return jax.ops.segment_sum(src, seg, n)
kernel_name = 'mk_perceiver_d1_seqx_r4_26162e'

def setup_inputs(seed: int=0):
    np.random.seed(seed)
    _w = jnp.asarray

    def _rec_inputs():
        import jax
        import jax.numpy as jnp
        _rk = jax.random.key(seed)
        x = 2.818e-05 + 1 * jax.random.normal(jax.random.fold_in(_rk, 1), (1, 128, 256), jnp.float32)
        _lenS = 128 - jax.random.randint(jax.random.fold_in(_rk, 7), (1,), 0, max(1, 128 // 4) + 1, jnp.int32)
        _lenS2 = 12544 - jax.random.randint(jax.random.fold_in(_rk, 8), (1,), 0, max(1, 12544 // 4) + 1, jnp.int32)
        _ctx_1024P = jax.random.normal(jax.random.fold_in(_rk, 11), (1, 16, 256), jnp.float32)
        _ctx_1024c = jax.random.dirichlet(jax.random.fold_in(_rk, 511), 0.3 * jnp.ones((16,), jnp.float32), (1, 12544))
        _ctx_1024t = jnp.einsum('bsk,bkd->bsd', _ctx_1024c, _ctx_1024P)
        _ctx_1024t = _ctx_1024t * jax.lax.rsqrt(jnp.mean(jnp.square(_ctx_1024t)) + 1e-12) * 0.953939
        ctx_1024 = -0.000392918 + 0.999932 * (_ctx_1024t + 0.3 * jax.random.normal(jax.random.fold_in(_rk, 611), (1, 12544, 256), jnp.float32))
        return (x, ctx_1024)
    x, ctx_1024 = _rec_inputs()

    def _L0_xattn_setup():
        import jax, jax.numpy as jnp
        import numpy as np
        key = jax.random.key(seed)
        k1, k2 = jax.random.split(key)
        B, S_ENC, S_DEC, D = (8, 512, 512, 256)
        enc_outputs = jax.random.normal(k1, (B, S_ENC, D), dtype=jnp.float32)
        dec_outputs = jax.random.normal(k2, (B, S_DEC, D), dtype=jnp.float32)
        return {'enc_outputs': enc_outputs, 'dec_outputs': dec_outputs}
    _L0_xattn_all = _L0_xattn_setup()
    _L0_xattn_in = {k: v for k, v in _L0_xattn_all.items() if k in ()}
    del _L0_xattn_all

    def _L0_attn_setup():
        import jax, jax.numpy as jnp
        import numpy as np
        import math
        N_HEAD = 16
        key = jax.random.key(seed)
        k1, k2, k3, k4, k5 = jax.random.split(key, 5)
        B, T, C = (8, 256, 256)
        scale = 0.02
        return {'x': jax.random.normal(k1, (B, T, C), dtype=jnp.float32), 'w_attn': jax.random.normal(k2, (C, 3 * C), dtype=jnp.float32) * scale, 'b_attn': jax.random.normal(k3, (3 * C,), dtype=jnp.float32) * scale, 'w_proj': jax.random.normal(k4, (C, C), dtype=jnp.float32) * scale, 'b_proj': jax.random.normal(k5, (C,), dtype=jnp.float32) * scale}
    _L0_attn_all = _L0_attn_setup()
    _L0_attn_in = {k: v for k, v in _L0_attn_all.items() if k in ('w_attn', 'b_attn', 'w_proj', 'b_proj')}
    del _L0_attn_all

    def _L0_ffn_setup():
        import jax, jax.numpy as jnp
        import numpy as np
        key = jax.random.key(seed)
        k1, k2, k3, k4, k5 = jax.random.split(key, 5)
        d_in, d_out, r = (256, 256, 32)
        x = jax.random.normal(k1, (8, 2048, d_in), dtype=jnp.float32)
        W = jax.random.normal(k2, (d_out, d_in), dtype=jnp.float32) * (1.0 / np.sqrt(d_in))
        b = jax.random.normal(k3, (d_out,), dtype=jnp.float32) * 0.01
        V_r = jax.random.normal(k4, (d_in, r), dtype=jnp.float32) * (1.0 / np.sqrt(d_in))
        C = jax.random.normal(k5, (d_out, r), dtype=jnp.float32) * (1.0 / np.sqrt(r))
        return {'x': x, 'W': W, 'b': b, 'V_r': V_r, 'C': C}
    _L0_ffn_all = _L0_ffn_setup()
    _L0_ffn_in = {k: v for k, v in _L0_ffn_all.items() if k in ('W', 'b', 'V_r', 'C')}
    del _L0_ffn_all
    return {'x': x, 'ctx_1024': ctx_1024, 'L0_attn_w_attn': _L0_attn_in['w_attn'], 'L0_attn_b_attn': _L0_attn_in['b_attn'], 'L0_attn_w_proj': _L0_attn_in['w_proj'], 'L0_attn_b_proj': _L0_attn_in['b_proj'], 'L0_ffn_W': _L0_ffn_in['W'], 'L0_ffn_b': _L0_ffn_in['b'], 'L0_ffn_V_r': _L0_ffn_in['V_r'], 'L0_ffn_C': _L0_ffn_in['C']}

def reference(x, ctx_1024, L0_attn_w_attn, L0_attn_b_attn, L0_attn_w_proj, L0_attn_b_proj, L0_ffn_W, L0_ffn_b, L0_ffn_V_r, L0_ffn_C):
    import jax
    import jax.numpy as jnp

    def _L0_xattn_ref(enc_outputs, dec_outputs):
        import jax, jax.numpy as jnp
        import numpy as np
        a_t = jnp.einsum('bed,btd->bet', enc_outputs, dec_outputs)
        a_t = jax.nn.softmax(a_t, axis=-1)
        c_t = jnp.einsum('bet,bed->btd', a_t, enc_outputs)
        return c_t

    def _L0_attn_ref(x, w_attn, b_attn, w_proj, b_proj):
        import jax, jax.numpy as jnp
        import numpy as np
        import math
        N_HEAD = 16
        B, T, C = x.shape
        H = N_HEAD
        hd = C // H
        qkv = jnp.einsum('btc,cd->btd', x, w_attn) + b_attn
        q, k, v = jnp.split(qkv, 3, axis=-1)

        def heads(t):
            return t.reshape(B, T, H, hd).transpose(0, 2, 1, 3)
        q, k, v = (heads(q), heads(k), heads(v))
        att = jnp.einsum('bhqd,bhkd->bhqk', q, k) * (1.0 / math.sqrt(hd))
        causal = jnp.tril(jnp.ones((T, T), dtype=bool))
        att = jnp.where(causal, att, jnp.float32(-jnp.inf))
        att = jax.nn.softmax(att, axis=-1)
        y = jnp.einsum('bhqk,bhkd->bhqd', att, v)
        y = y.transpose(0, 2, 1, 3).reshape(B, T, C)
        return jnp.einsum('btc,cd->btd', y, w_proj) + b_proj

    def _L0_ffn_ref(x, W, b, V_r, C):
        import jax, jax.numpy as jnp
        import numpy as np
        base = jnp.einsum('bsd,od->bso', x, W) + b
        correction = jnp.einsum('bsr,or->bso', jnp.einsum('bsd,dr->bsr', x, V_r), C)
        return base + correction
    x = x + _L0_xattn_ref(ctx_1024, _layernorm(x, axis=-1))
    x = x + _L0_attn_ref(_layernorm(x, axis=-1), L0_attn_w_attn, L0_attn_b_attn, L0_attn_w_proj, L0_attn_b_proj)
    x = x + _L0_ffn_ref(_layernorm(x, axis=-1), L0_ffn_W, L0_ffn_b, L0_ffn_V_r, L0_ffn_C)
    return x

_drawn_inputs = setup_inputs


def setup_inputs(seed=0):
    import zlib

    import numpy as np

    out = dict(_drawn_inputs(seed))
    spreads = {}
    factors = {'L0_attn_w_attn': 8.0,
     'L0_attn_b_attn': 8.0,
     'L0_attn_w_proj': 8.0,
     'L0_attn_b_proj': 61.369,
     'L0_ffn_W': 8.0,
     'L0_ffn_b': 64.0,
     'L0_ffn_V_r': 8.0,
     'L0_ffn_C': 8.0}
    for name, (base, spread) in spreads.items():
        noise = np.random.default_rng([zlib.crc32(name.encode()), seed]).standard_normal(out[name].shape)
        drawn = base * np.exp(spread * noise) if base else spread * noise
        out[name] = jnp.asarray(drawn.astype(out[name].dtype))
    for name, factor in factors.items():
        out[name] = (out[name] * factor).astype(out[name].dtype)
    return out
```

```python
from contextlib import ExitStack

import concourse.bass as bass
from concourse import mybir

F32 = mybir.dt.float32
BF16 = mybir.dt.bfloat16
ALU = mybir.AluOpType
ACT = mybir.ActivationFunctionType
AX_X = mybir.AxisListType.X

P = 128
NHEAD = 16
EPS = 1e-5
MASKED = -1e30

STEP = 2
UNROLL = 8
CHUNK = 4
RING = STEP * UNROLL
SLOTS = RING // CHUNK
LAG = 2


def perceiver_kernel(nc, x, ctx_rows, ctx_cols, w_qk, b_qk, w_v, b_v, w_proj, b_proj,
                     w_ffn, b_ffn, v_r, c_t, out):
    T, D = x.shape
    DC = D // P
    TILES = ctx_rows.shape[1] // D
    STEPS = TILES // STEP
    LOADS = -(-TILES // CHUNK)
    HD = D // NHEAD
    GROUPS = 4
    HM = NHEAD // GROUPS
    R = v_r.shape[-1]
    HA = HD + 1
    assert T == P and TILES % STEP == 0 and RING % CHUNK == 0

    with ExitStack() as ctx:
        def sb(name, shape, dt=F32):
            return ctx.enter_context(nc.sbuf_tensor(name, shape, dt))

        def psum(name, shape):
            return ctx.enter_context(nc.psum_tensor(name, shape, F32))

        def sem(name):
            return ctx.enter_context(nc.semaphore(name))

        x0 = sb("x0", [P, D])
        x1 = sb("x1", [P, D])
        x2 = sb("x2", [P, D])
        x3 = sb("x3", [P, D])
        normed = sb("normed", [P, D])
        normed_t = sb("normed_t", [P, DC, P])
        query_t = sb("query_t", [P, DC, P])
        bn = sb("bn", [P, 6])
        mean_var = sb("mean_var", [P, 2])
        var_eps = sb("var_eps", [P, 1])
        minus_half = sb("minus_half", [P, 1])
        rstd = sb("rstd", [P, 1])
        rows_ring = sb("rows_ring", [P, RING, D])
        cols_ring = sb("cols_ring", [P, RING, DC, P])
        neg_max = sb("neg_max", [P, 2, STEP])
        exps = sb("exps", [P, 2, STEP, P])
        sums = sb("sums", [P, 2, STEP])
        inv_sums = sb("inv_sums", [P, 2, STEP])
        probs = sb("probs", [P, 2, STEP, P])
        ident = sb("ident", [P, P])
        ident_bf = sb("ident_bf", [P, P], BF16)
        mask = sb("mask", [P, P], BF16)
        ones = sb("ones", [1, P])
        blocks = sb("blocks", [HM, HM, P])
        wqk_sb = sb("wqk_sb", [P, DC, 2 * HM, P])
        bqk_sb = sb("bqk_sb", [HM, 2, P])
        wv_sb = sb("wv_sb", [P, DC, D])
        bv_sb = sb("bv_sb", [1, D])
        wproj_sb = sb("wproj_sb", [P, DC, D])
        bproj_sb = sb("bproj_sb", [1, D])
        wffn_sb = sb("wffn_sb", [P, DC, D])
        bffn_sb = sb("bffn_sb", [1, D])
        vr_sb = sb("vr_sb", [P, DC, R])
        ct_sb = sb("ct_sb", [R, D])
        q_t = sb("q_t", [P, HM, P])
        k_t = sb("k_t", [P, HM, P])
        v_ones = sb("v_ones", [P, NHEAD, HA])
        head_max = sb("head_max", [P, GROUPS, HM])
        shifted = sb("shifted", [P, GROUPS, HM, P])
        head_exp = sb("head_exp", [P, GROUPS, HM, P])
        head_exp_t = sb("head_exp_t", [P, GROUPS, HM, P])
        head_inv = sb("head_inv", [P, NHEAD])
        y = sb("y", [P, NHEAD, HD])
        y_t = sb("y_t", [P, DC, P])
        low_t = sb("low_t", [R, P])

        bank = [psum(f"bank{i}", [P, 512]) for i in range(8)]
        scores = [bank[0], bank[1]]
        weighted = bank[2]
        turn = bank[5]
        head_scores = [bank[0], bank[1], bank[3], bank[4]]
        q_ps, k_ps, v_ps = bank[7], bank[6], bank[2]
        exp_t_ps = [bank[7], bank[6]]
        y_ps = bank[2]
        proj_ps, low_ps, ffn_ps = bank[3], bank[0], bank[4]

        x_landed = sem("x_landed")
        rows_landed = [sem(f"rows_landed{i}") for i in range(SLOTS)]
        cols_landed = [sem(f"cols_landed{i}") for i in range(SLOTS)]
        weights_landed = sem("weights_landed")
        consts_ready = sem("consts_ready")
        pool_step = sem("pool_step")
        dve_step = sem("dve_step")
        stats_ready = sem("stats_ready")
        rstd_ready = sem("rstd_ready")
        normed_ready = sem("normed_ready")
        turned = sem("turned")
        turn_copied = sem("turn_copied")
        scores_ready = sem("scores_ready")
        max_ready = sem("max_ready")
        exps_ready = sem("exps_ready")
        probs_ready = sem("probs_ready")
        summed = sem("summed")
        x1_ready = sem("x1_ready")
        qkv_ready = sem("qkv_ready")
        q_copied = sem("q_copied")
        k_copied = sem("k_copied")
        v_copied = sem("v_copied")
        head_scores_ready = sem("head_scores_ready")
        shifted_ready = sem("shifted_ready")
        head_exp_ready = sem("head_exp_ready")
        exp_turned = sem("exp_turned")
        exp_t_dve = sem("exp_t_dve")
        exp_t_act = sem("exp_t_act")
        y_summed = sem("y_summed")
        y_ready = sem("y_ready")
        y_turned = sem("y_turned")
        y_t_copied = sem("y_t_copied")
        proj_ready = sem("proj_ready")
        low_ready = sem("low_ready")
        low_copied = sem("low_copied")
        ffn_ready = sem("ffn_ready")
        x3_ready = sem("x3_ready")
        out_stored = sem("out_stored")

        weights = [(wqk_sb, w_qk), (bqk_sb, b_qk), (wv_sb, w_v), (bv_sb, b_v),
                   (wproj_sb, w_proj), (bproj_sb, b_proj), (wffn_sb, w_ffn), (bffn_sb, b_ffn),
                   (vr_sb, v_r), (ct_sb, c_t)]
        NCONSTS = 7

        block = ctx.enter_context(nc.Block())

        LOOPS = (STEPS - LAG) // UNROLL

        def pipeline(eng, step):
            for s in range(LAG):
                step(s, s)
            with eng.Fori(0, LOOPS) as i:
                for k in range(UNROLL):
                    step((LAG + k) % UNROLL, UNROLL * i + (LAG + k))
            for s in range(LAG + LOOPS * UNROLL, STEPS + LAG):
                step(s % UNROLL, s)

        @block.sync
        def _(sp):
            def load(slot, first, count):
                ring = slice(slot * CHUNK, slot * CHUNK + count)
                sp.dma_start(cols_ring[:, ring].rearrange("p t c e -> p (t c e)"),
                             ctx_cols[:, bass.ds(first * D, count * D)]).then_inc(cols_landed[slot], 16)
                sp.dma_start(rows_ring[:, ring].rearrange("p t d -> p (t d)"),
                             ctx_rows[:, bass.ds(first * D, count * D)]).then_inc(rows_landed[slot], 16)

            for n in range(SLOTS):
                load(n, n * CHUNK, CHUNK)
            for dst, src in weights:
                sp.dma_start(dst[:], src).then_inc(weights_landed, 16)
            full = TILES // CHUNK // SLOTS
            with sp.Fori(1, full) as i:
                for slot in range(SLOTS):
                    sp.wait_ge(summed, i * UNROLL + (slot * CHUNK // STEP - UNROLL + CHUNK // STEP))
                    load(slot, i * RING + slot * CHUNK, CHUNK)
            for n in range(full * SLOTS, LOADS):
                sp.wait_ge(summed, (n - SLOTS + 1) * CHUNK // STEP)
                load(n % SLOTS, n * CHUNK, min(CHUNK, TILES - n * CHUNK))
            sp.wait_ge(x3_ready, 1)
            sp.dma_start(out, x3[:]).then_inc(out_stored, 16)
            sp.wait_ge(out_stored, 16)

        @block.gpsimd
        def _(pool):
            pool.memset(ident[:], 0.0).then_inc(pool_step, 1)
            pool.memset(ident_bf[:], 0.0).then_inc(pool_step, 1)
            pool.memset(mask[:], 0.0).then_inc(pool_step, 1)
            pool.memset(blocks[:], 1.0).then_inc(pool_step, 1)
            pool.memset(minus_half[:], -0.5).then_inc(consts_ready, 1)
            pool.memset(ones[:], 1.0).then_inc(consts_ready, 1)
            pool.memset(v_ones[:], 1.0).then_inc(consts_ready, 1)
            pool.wait_ge(pool_step, 4)
            pool.affine_select(out=ident[:], in_=ident[:], compare_op=ALU.not_equal, fill=1.0, base=0,
                               pattern=[[-1, P]], channel_multiplier=1).then_inc(consts_ready, 1)
            pool.affine_select(out=ident_bf[:], in_=ident_bf[:], compare_op=ALU.not_equal, fill=1.0, base=0,
                               pattern=[[-1, P]], channel_multiplier=1).then_inc(consts_ready, 1)
            pool.affine_select(out=mask[:], in_=mask[:], compare_op=ALU.is_ge, fill=MASKED, base=0,
                               pattern=[[-1, P]], channel_multiplier=1).then_inc(consts_ready, 1)
            pool.affine_select(out=blocks[:], in_=blocks[:], compare_op=ALU.is_equal, fill=0.0, base=0,
                               pattern=[[-1, HM], [0, P]], channel_multiplier=1).then_inc(consts_ready, 1)
            pool.wait_ge(consts_ready, NCONSTS)
            for n in range(3):
                pool.wait_ge(stats_ready, n + 1)
                pool.tensor_tensor(rstd[:], var_eps[:], minus_half[:], ALU.pow).then_inc(rstd_ready, 1)

        @block.tensor
        def _(pe):
            def turn_normed(n):
                pe.wait_ge(normed_ready, n + 1)
                for c in range(DC):
                    last = pe.transpose(turn[:, c * P:(c + 1) * P], normed[:, c * P:(c + 1) * P], ident[:])
                last.then_inc(turned, 1)

            def step(k, s):
                static = isinstance(s, int)
                if not static or s < STEPS:
                    if k % (CHUNK // STEP) == 0:
                        slot = k * STEP // CHUNK
                        pe.wait_ge(cols_landed[slot], 16 * (s // UNROLL + 1) if static
                                   else 2 * s + (16 - 2 * k))
                    if not static or s >= 2:
                        pe.wait_ge(exps_ready, s - 1)
                    for t in range(STEP):
                        for c in range(DC):
                            last = pe.matmul(scores[k % 2][:, t * P:(t + 1) * P],
                                             cols_ring[:, k * STEP + t, c, :], query_t[:, c, :],
                                             start=(c == 0), stop=(c == DC - 1))
                    last.then_inc(scores_ready, 1)
                if not static or s >= LAG:
                    b = (k - LAG) % UNROLL
                    if b % (CHUNK // STEP) == 0:
                        slot = b * STEP // CHUNK
                        pe.wait_ge(rows_landed[slot], 16 * ((s - LAG) // UNROLL + 1) if static
                                   else 2 * s + (16 - 2 * LAG - 2 * b))
                    pe.wait_ge(probs_ready, s - LAG + 1)
                    for t in range(STEP):
                        last = pe.matmul(weighted[:, 0:D], probs[:, b % 2, t, :],
                                         rows_ring[:, b * STEP + t, :],
                                         start=False,
                                         stop=(static and s == STEPS + LAG - 1 and t == STEP - 1),
                                         skip_group_check=True)
                    last.then_inc(summed, 1)

            pe.wait_ge(consts_ready, NCONSTS)
            turn_normed(0)
            pe.matmul(weighted[:, 0:D], ident[:], x0[:], start=True, stop=False, skip_group_check=True)
            pe.wait_ge(turn_copied, 1)
            pipeline(pe, step)

            pe.wait_ge(weights_landed, 16 * len(weights))
            pe.wait_ge(exps_ready, STEPS)
            for j in range(GROUPS):
                pe.matmul(head_scores[j][:], ident_bf[:], mask[:].unsqueeze(1).to_broadcast([P, HM, P]),
                          start=True, stop=False, skip_group_check=True)
            for i, ps in enumerate((q_ps, k_ps)):
                pe.matmul(ps[:], bqk_sb[:, i, :], blocks[:].rearrange("p m t -> p (m t)"),
                          start=True, stop=False, skip_group_check=True)
            pe.wait_ge(x1_ready, 1)
            pe.matmul(v_ps[:, 0:D], ones[:], bv_sb[:], start=True, stop=False, skip_group_check=True)
            turn_normed(1)
            pe.wait_ge(turn_copied, 2)
            for i, ps in enumerate((q_ps, k_ps)):
                for m in range(HM):
                    for c in range(DC):
                        last = pe.matmul(ps[:, m * P:(m + 1) * P], wqk_sb[:, c, i * HM + m, :], normed_t[:, c, :],
                                         start=False, stop=(c == DC - 1), skip_group_check=True)
                last.then_inc(qkv_ready, 1)
            for c in range(DC):
                last = pe.matmul(v_ps[:, 0:D], normed_t[:, c, :], wv_sb[:, c, :], start=False,
                                 stop=(c == DC - 1), skip_group_check=True)
            last.then_inc(qkv_ready, 1)
            pe.wait_ge(q_copied, 1)
            pe.wait_ge(k_copied, 1)
            for j in range(GROUPS):
                rows = slice(32 * j, 32 * j + HD)
                for m in range(HM):
                    last = pe.matmul(head_scores[j][:, m * P:(m + 1) * P], q_t[rows, m, :], k_t[rows, m, :],
                                     start=False, stop=True, skip_group_check=True)
                last.then_inc(head_scores_ready, 1)

            def weigh_values(j):
                if j % 2 == 0:
                    pe.wait_ge(exp_t_dve, j // 2 + 1)
                else:
                    pe.wait_ge(exp_t_act, j // 2 + 1)
                if j == 0:
                    pe.wait_ge(v_copied, 1)
                for m in range(HM):
                    h = m * GROUPS + j
                    last = pe.matmul(y_ps[:, h * HA:(h + 1) * HA], head_exp_t[:, j, m, :], v_ones[:, h, :],
                                     start=True, stop=True, skip_group_check=True)
                last.then_inc(y_summed, 1)

            for j in range(GROUPS):
                pe.wait_ge(head_exp_ready, j + 1)
                if j >= 2:
                    pe.wait_ge(exp_t_dve if j % 2 == 0 else exp_t_act, j // 2)
                for m in range(HM):
                    last = pe.transpose(exp_t_ps[j % 2][:, m * P:(m + 1) * P], head_exp[:, j, m, :], ident[:])
                last.then_inc(exp_turned, 1)
                if j >= 1:
                    weigh_values(j - 1)
            weigh_values(GROUPS - 1)
            pe.wait_ge(shifted_ready, GROUPS)
            pe.matmul(proj_ps[:, 0:D], ones[:], bproj_sb[:], start=True, stop=False, skip_group_check=True)
            pe.matmul(ffn_ps[:, 0:D], ones[:], bffn_sb[:], start=True, stop=False, skip_group_check=True)
            pe.wait_ge(y_ready, 1)
            for c in range(DC):
                last = pe.transpose(turn[:, c * P:(c + 1) * P],
                                    y[:].rearrange("p h d -> p (h d)")[:, c * P:(c + 1) * P], ident[:])
            last.then_inc(y_turned, 1)
            pe.wait_ge(y_t_copied, 1)
            for c in range(DC):
                last = pe.matmul(proj_ps[:, 0:D], y_t[:, c, :], wproj_sb[:, c, :], start=False,
                                 stop=(c == DC - 1), skip_group_check=True)
            last.then_inc(proj_ready, 1)
            turn_normed(2)
            pe.wait_ge(turn_copied, 3)
            for c in range(DC):
                last = pe.matmul(low_ps[0:R, 0:P], vr_sb[:, c, :], normed_t[:, c, :], start=(c == 0),
                                 stop=(c == DC - 1))
            last.then_inc(low_ready, 1)
            for c in range(DC):
                pe.matmul(ffn_ps[:, 0:D], normed_t[:, c, :], wffn_sb[:, c, :], start=False, stop=False,
                          skip_group_check=True)
            pe.wait_ge(low_copied, 1)
            pe.matmul(ffn_ps[:, 0:D], low_t[:], ct_sb[:], start=False, stop=True,
                      skip_group_check=True).then_inc(ffn_ready, 1)

        @block.scalar
        def _(act):
            act.dma_start(x0[:], x).then_inc(x_landed, 16)

            def exp_step(k, s):
                static = isinstance(s, int)
                if static and s >= STEPS:
                    return
                b = k % 2
                act.wait_ge(max_ready, s + 1)
                if not static or s >= 2:
                    act.wait_ge(probs_ready, s - 1)
                for t in range(STEP):
                    last = act.activation(exps[:, b, t, :], scores[b][:, t * P:(t + 1) * P], ACT.Exp,
                                          bias=neg_max[:, b, t:t + 1], accum_out=sums[:, b, t:t + 1])
                last.then_inc(exps_ready, 1)

            pipeline(act, exp_step)

            act.wait_ge(qkv_ready, 2)
            act.copy(k_t[:].rearrange("p m t -> p (m t)"), k_ps[:]).then_inc(k_copied, 1)
            act.wait_ge(qkv_ready, 3)
            act.copy(v_ones[:, :, 0:HD], v_ps[:, 0:D].rearrange("p (h d) -> p h d", h=NHEAD)).then_inc(v_copied, 1)

            def copy_exp_t(j):
                act.wait_ge(exp_turned, j + 1)
                act.copy(head_exp_t[:, j].rearrange("p m q -> p (m q)"), exp_t_ps[j % 2][:]).then_inc(exp_t_act, 1)

            for j in range(GROUPS):
                act.wait_ge(shifted_ready, j + 1)
                act.activation(head_exp[:, j], shifted[:, j], ACT.Exp, scale=float(HD) ** -0.5)\
                   .then_inc(head_exp_ready, 1)
                if j == 2:
                    copy_exp_t(1)
            copy_exp_t(3)
            act.wait_ge(low_ready, 1)
            act.copy(low_t[:], low_ps[0:R, 0:P]).then_inc(low_copied, 1)

        @block.vector
        def _(dve):
            link_count = [0]

            def link(ins):
                link_count[0] += 1
                ins.then_inc(dve_step, 1)
                dve.wait_ge(dve_step, link_count[0])

            def layer_norm(n, src):
                link(dve.bn_stats(bn[:], src[:]))
                link(dve.bn_aggr(mean_var[:], bn[:]))
                dve.tensor_scalar(var_eps[:], mean_var[:, 1:2], EPS, None, ALU.add).then_inc(stats_ready, 1)
                dve.wait_ge(rstd_ready, n + 1)
                dve.tensor_scalar(normed[:], src[:], mean_var[:, 0:1], rstd[:, 0:1], ALU.subtract, ALU.mult)\
                   .then_inc(normed_ready, 1)

            def copy_turn(n, dst):
                dve.wait_ge(turned, n + 1)
                dve.tensor_copy(dst[:].rearrange("p c t -> p (c t)"), turn[:, 0:D]).then_inc(turn_copied, 1)

            dve.wait_ge(x_landed, 16)
            layer_norm(0, x0)
            copy_turn(0, query_t)
            links_before = link_count[0]

            def step(k, s):
                static = isinstance(s, int)
                if not static or s < STEPS:
                    b = k % 2
                    dve.wait_ge(scores_ready, s + 1)
                    dve.tensor_reduce(neg_max[:, b, :], scores[b][:, 0:STEP * P].rearrange("p (t q) -> p t q", q=P),
                                      AX_X, ALU.max, negate=True).then_inc(max_ready, 1)
                if (not static or s >= 1) and not (static and s > STEPS):
                    b = (k - 1) % 2
                    dve.wait_ge(exps_ready, s)
                    dve.reciprocal(inv_sums[:, b, :], sums[:, b, :]).then_inc(dve_step, 1)
                    if not static or s >= 3:
                        dve.wait_ge(summed, s - 2)
                    dve.wait_ge(dve_step, s + links_before)
                    for t in range(STEP):
                        last = dve.tensor_scalar(probs[:, b, t, :], exps[:, b, t, :], inv_sums[:, b, t:t + 1],
                                                 None, ALU.mult)
                    last.then_inc(probs_ready, 1)

            pipeline(dve, step)
            link_count[0] += STEPS

            dve.wait_ge(summed, STEPS)
            dve.tensor_copy(x1[:], weighted[:, 0:D]).then_inc(x1_ready, 1)
            dve.wait_ge(x1_ready, 1)
            layer_norm(1, x1)
            copy_turn(1, normed_t)
            dve.wait_ge(qkv_ready, 1)
            dve.tensor_copy(q_t[:].rearrange("p m t -> p (m t)"), q_ps[:]).then_inc(q_copied, 1)

            def copy_exp_t(j):
                dve.wait_ge(exp_turned, j + 1)
                dve.tensor_copy(head_exp_t[:, j].rearrange("p m q -> p (m q)"), exp_t_ps[j % 2][:])\
                   .then_inc(exp_t_dve, 1)

            for j in range(GROUPS):
                dve.wait_ge(head_scores_ready, j + 1)
                s_view = head_scores[j][:].rearrange("p (m k) -> p m k", k=P)
                link(dve.tensor_reduce(head_max[:, j, :], s_view, AX_X, ALU.max))
                dve.tensor_tensor(shifted[:, j], s_view, head_max[:, j, :].unsqueeze(2).to_broadcast([P, HM, P]),
                                  ALU.subtract).then_inc(shifted_ready, 1)
                if j == 2:
                    copy_exp_t(0)
            copy_exp_t(2)
            dve.wait_ge(y_summed, GROUPS)
            y_view = y_ps[:, 0:NHEAD * HA].rearrange("p (h a) -> p h a", a=HA)
            link(dve.reciprocal(head_inv[:], y_view[:, :, HD]))
            dve.tensor_tensor(y[:], y_view[:, :, 0:HD], head_inv[:].unsqueeze(2).to_broadcast([P, NHEAD, HD]),
                              ALU.mult).then_inc(y_ready, 1)
            dve.wait_ge(y_turned, 1)
            dve.tensor_copy(y_t[:].rearrange("p c t -> p (c t)"), turn[:, 0:D]).then_inc(y_t_copied, 1)
            dve.wait_ge(proj_ready, 1)
            link(dve.tensor_tensor(x2[:], proj_ps[:, 0:D], x1[:], ALU.add))
            layer_norm(2, x2)
            copy_turn(2, normed_t)
            dve.wait_ge(ffn_ready, 1)
            dve.tensor_tensor(x3[:], ffn_ps[:, 0:D], x2[:], ALU.add).then_inc(x3_ready, 1)


def kernel(**inputs):
    import numpy as np
    import concourse.bacc as bacc
    from concourse import mybir as mb
    from concourse.bass_utils import run_bass_kernel_spmd

    x = np.asarray(inputs["x"])[0]
    context = np.asarray(inputs["ctx_1024"])[0]
    w_attn = np.asarray(inputs["L0_attn_w_attn"])
    b_attn = np.asarray(inputs["L0_attn_b_attn"])
    D = x.shape[1]
    DC, TILES, HD, GROUPS, HM = D // P, context.shape[0] // P, D // NHEAD, 4, NHEAD // 4

    def chunked(w):
        return np.ascontiguousarray(w.reshape(-1, P, w.shape[-1]).transpose(1, 0, 2))

    def padded(w):
        heads = w[:, 0:2 * D].reshape(-1, 2 * HM, GROUPS, HD)
        return np.pad(heads, ((0, 0), (0, 0), (0, 0), (0, 32 - HD))).reshape(-1, 2 * HM * P)

    tiles = context.reshape(TILES, P, DC, P)
    arrays = {
        "x": x,
        "ctx_rows": tiles.transpose(1, 0, 2, 3).reshape(P, TILES * D),
        "ctx_cols": tiles.transpose(3, 0, 2, 1).reshape(P, TILES * D),
        "w_qk": chunked(padded(w_attn)).reshape(P, DC, 2 * HM, P),
        "b_qk": padded(b_attn[None]).reshape(2, HM, P).transpose(1, 0, 2),
        "w_v": chunked(w_attn[:, 2 * D:]),
        "b_v": b_attn[None, 2 * D:],
        "w_proj": chunked(np.asarray(inputs["L0_attn_w_proj"])),
        "b_proj": np.asarray(inputs["L0_attn_b_proj"])[None],
        "w_ffn": chunked(np.asarray(inputs["L0_ffn_W"]).T),
        "b_ffn": np.asarray(inputs["L0_ffn_b"])[None],
        "v_r": chunked(np.asarray(inputs["L0_ffn_V_r"])),
        "c_t": np.asarray(inputs["L0_ffn_C"]).T,
    }
    arrays = {f"{name}_dram": np.ascontiguousarray(a) for name, a in arrays.items()}
    nc = bacc.Bacc("TRN2", target_bir_lowering=False, num_devices=1)
    args = [nc.dram_tensor(name, a.shape, mb.dt.from_np(a.dtype), kind="ExternalInput").ap()
            for name, a in arrays.items()]
    out = nc.dram_tensor("out_dram", x.shape, mb.dt.from_np(x.dtype), kind="ExternalOutput").ap()
    perceiver_kernel(nc, *args, out)
    result = run_bass_kernel_spmd(nc, [arrays], core_ids=[0])
    return result.results[0]["out_dram"][None]
```

```python
from contextlib import ExitStack

import concourse.bass as bass
from concourse import mybir

F32 = mybir.dt.float32
F32R = mybir.dt.float32r
BF16 = mybir.dt.bfloat16
ALU = mybir.AluOpType
ACT = mybir.ActivationFunctionType
AX_X = mybir.AxisListType.X

P = 128
NHEAD = 16
EPS = 1e-5
MASKED = -1e30

STEP = 2
UNROLL = 8
CHUNK = 4
RING = STEP * UNROLL
SLOTS = RING // CHUNK
LAG = 3
PEELED = 4
SPLITS = 4


def perceiver_kernel(nc, x, ctx_rows, ctx_cols, w_qk, b_qk, w_v, b_v, w_proj, b_proj,
                     w_ffn, b_ffn, v_r, c_t, out):
    T, D = x.shape
    DC = D // P
    TILES = ctx_rows.shape[1] // D
    STEPS = TILES // STEP
    LOADS = -(-TILES // CHUNK)
    HD = D // NHEAD
    GROUPS = 4
    HM = NHEAD // GROUPS

    def head_of(j, m):
        return (m // 2) * (NHEAD // DC) + 2 * j + m % 2
    R = v_r.shape[-1]
    HA = HD + 1
    SCALE = float(HD) ** -0.5
    assert T == P and TILES % STEP == 0 and RING % CHUNK == 0

    with ExitStack() as ctx:
        def sb(name, shape, dt=F32):
            return ctx.enter_context(nc.sbuf_tensor(name, shape, dt))

        def psum(name, shape):
            return ctx.enter_context(nc.psum_tensor(name, shape, F32))

        def sem(name):
            return ctx.enter_context(nc.semaphore(name))

        x0 = sb("x0", [P, D])
        x1 = sb("x1", [P, D])
        x2 = sb("x2", [P, D])
        x1_bias = sb("x1_bias", [P, D])
        x2_bias = sb("x2_bias", [P, D])
        x3 = sb("x3", [P, D])
        normed = sb("normed", [P, D])
        normed_t = sb("normed_t", [P, DC, P])
        query_t = sb("query_t", [P, DC, P])
        bn = sb("bn", [P, 6])
        mean_var = sb("mean_var", [P, 2])
        var_eps = sb("var_eps", [P, 1])
        zeros = sb("zeros", [P, P])
        minus_half = sb("minus_half", [P, 1])
        rstd = sb("rstd", [P, 1])
        rows_ring = sb("rows_ring", [P, RING, D])
        cols_ring = sb("cols_ring", [P, RING, DC, P])
        neg_max = sb("neg_max", [P, 2, STEP])
        exps = sb("exps", [P, 2, STEP, P])
        sums = sb("sums", [P, 2, STEP])
        inv_sums = sb("inv_sums", [P, 2, STEP])
        probs = sb("probs", [P, SPLITS, STEP, 2, P], F32R)
        rows_split = sb("rows_split", [P, SPLITS, STEP, 2, D], F32R)
        ident = sb("ident", [P, P])
        ident_bf = sb("ident_bf", [P, P], BF16)
        mask = sb("mask", [P, P], BF16)
        warm = sb("warm", [P, 512], BF16)
        ones = sb("ones", [1, P])
        in_head = sb("in_head", [P, P // HD])
        parity = sb("parity", [P, 2])
        wqk_sb = sb("wqk_sb", [P, DC, 2 * DC, P])
        bqk_sb = sb("bqk_sb", [P, 2 * DC])
        wv_sb = sb("wv_sb", [P, DC, D])
        bv_sb = sb("bv_sb", [1, D])
        wproj_sb = sb("wproj_sb", [P, DC, D])
        bproj_sb = sb("bproj_sb", [P, D])
        wffn_sb = sb("wffn_sb", [P, DC, D])
        bffn_sb = sb("bffn_sb", [P, D])
        vr_sb = sb("vr_sb", [P, DC, R])
        ct_sb = sb("ct_sb", [R, D])
        q_t = sb("q_t", [P, DC, P])
        k_t = sb("k_t", [P, DC, 2, P])
        v_ones = sb("v_ones", [P, NHEAD, HA])
        head_max = sb("head_max", [P, GROUPS, HM])
        shifted = sb("shifted", [P, GROUPS, HM, P])
        head_exp = sb("head_exp", [P, GROUPS, HM, P])
        head_exp_t = sb("head_exp_t", [P, GROUPS, HM, P])
        head_inv = sb("head_inv", [P, NHEAD])
        y = sb("y", [P, NHEAD, HD])
        y_t = sb("y_t", [P, DC, P])
        low_t = sb("low_t", [R, P])

        bank = [psum(f"bank{i}", [P, 512]) for i in range(8)]
        scores = [bank[0], bank[1]]
        weighted = bank[2]
        turn = bank[5]
        head_scores = [bank[0], bank[1], bank[3], bank[4]]
        q_ps, k_ps, v_ps = bank[7], [bank[6], bank[5]], bank[2]
        exp_t_ps = [bank[7], bank[6], bank[5], bank[0]]
        y_ps = bank[2]
        proj_ps, low_ps, ffn_ps = bank[3], bank[0], bank[4]

        x_landed = sem("x_landed")
        warm_ready = sem("warm_ready")
        rows_landed = [sem(f"rows_landed{i}") for i in range(SLOTS)]
        cols_landed = [sem(f"cols_landed{i}") for i in range(SLOTS)]
        weights_landed = sem("weights_landed")
        consts_ready = sem("consts_ready")
        pool_step = sem("pool_step")
        dve_step = sem("dve_step")
        stats_ready = sem("stats_ready")
        rstd_ready = sem("rstd_ready")
        normed_ready = sem("normed_ready")
        turned = sem("turned")
        turn_copied = sem("turn_copied")
        scores_ready = sem("scores_ready")
        max_ready = sem("max_ready")
        exps_ready = sem("exps_ready")
        probs_high = sem("probs_high")
        probs_ready = sem("probs_ready")
        rows_high = sem("rows_high")
        rows_ready = sem("rows_ready")
        summed = sem("summed")
        x1_ready = sem("x1_ready")
        x1_bias_ready = sem("x1_bias_ready")
        x2_ready = sem("x2_ready")
        x2_bias_ready = sem("x2_bias_ready")
        q_ready = sem("q_ready")
        k_ready = sem("k_ready")
        v_ready = sem("v_ready")
        q_copied = sem("q_copied")
        k_copied = sem("k_copied")
        parity_ready = sem("parity_ready")
        v_copied = sem("v_copied")
        head_scores_ready = sem("head_scores_ready")
        head_max_ready = sem("head_max_ready")
        shifted_ready = sem("shifted_ready")
        head_exp_ready = sem("head_exp_ready")
        exp_turned = sem("exp_turned")
        exp_t_copied = [sem(f"exp_t_copied{j}") for j in range(GROUPS)]
        y_summed = sem("y_summed")
        y_ready = sem("y_ready")
        y_turned = sem("y_turned")
        y_t_copied = sem("y_t_copied")
        proj_ready = sem("proj_ready")
        low_ready = sem("low_ready")
        low_copied = sem("low_copied")
        ffn_ready = sem("ffn_ready")
        x3_ready = sem("x3_ready")
        out_stored = sem("out_stored")

        weights = [(wqk_sb, w_qk), (bqk_sb, b_qk), (wv_sb, w_v), (bv_sb, b_v),
                   (wproj_sb, w_proj), (bproj_sb, b_proj.to_broadcast([P, D])), (wffn_sb, w_ffn), (bffn_sb, b_ffn.to_broadcast([P, D])),
                   (vr_sb, v_r), (ct_sb, c_t)]
        NCONSTS = 8

        WARM_START, WARM_X, WARM_NORM1, WARM_HEADS, WARM_Y, WARM_NORM2 = 4, 2, 10, 2, 1, 4

        block = ctx.enter_context(nc.Block())

        LOOPS = (STEPS - PEELED) // UNROLL

        def pipeline(eng, step):
            for s in range(PEELED):
                step(s, s)
            with eng.Fori(0, LOOPS) as i:
                for k in range(UNROLL):
                    step((PEELED + k) % UNROLL, UNROLL * i + (PEELED + k))
            for s in range(PEELED + LOOPS * UNROLL, STEPS + LAG):
                step(s % UNROLL, s)

        @block.sync
        def _(sp):
            sp.dma_start(x0[:], x).then_inc(x_landed, 16)

            def load(slot, first, count, used):
                ring = slice(slot * CHUNK, slot * CHUNK + count)
                if used is not None:
                    sp.wait_ge(scores_ready, used)
                sp.dma_start(cols_ring[:, ring].rearrange("p t c e -> p (t c e)"),
                             ctx_cols[:, bass.ds(first * D, count * D)]).then_inc(cols_landed[slot], 16)
                if used is not None:
                    sp.wait_ge(rows_ready, used)
                sp.dma_start(rows_ring[:, ring].rearrange("p t d -> p (t d)"),
                             ctx_rows[:, bass.ds(first * D, count * D)]).then_inc(rows_landed[slot], 16)

            for n in range(SLOTS):
                load(n, n * CHUNK, CHUNK, None)
            full = TILES // CHUNK // SLOTS
            with sp.Fori(1, full) as i:
                for slot in range(SLOTS):
                    load(slot, i * RING + slot * CHUNK, CHUNK,
                         i * UNROLL + (slot * CHUNK // STEP - UNROLL + CHUNK // STEP))
            for n in range(full * SLOTS, LOADS):
                load(n % SLOTS, n * CHUNK, min(CHUNK, TILES - n * CHUNK), (n - SLOTS + 1) * CHUNK // STEP)
            for dst, src in weights:
                sp.dma_start(dst[:], src).then_inc(weights_landed, 16)
            sp.wait_ge(x3_ready, 1)
            sp.dma_start(out, x3[:]).then_inc(out_stored, 16)
            sp.wait_ge(out_stored, 16)

        @block.gpsimd
        def _(pool):
            pool.memset(ident[:], 0.0).then_inc(pool_step, 1)
            pool.memset(ident_bf[:], 0.0).then_inc(pool_step, 1)
            pool.memset(mask[:], 0.0).then_inc(pool_step, 1)
            pool.memset(in_head[:], 1.0).then_inc(pool_step, 1)
            pool.memset(minus_half[:], -0.5).then_inc(consts_ready, 1)
            pool.memset(ones[:], 1.0).then_inc(consts_ready, 1)
            pool.memset(zeros[:], 0.0).then_inc(consts_ready, 1)
            pool.memset(v_ones[:], 1.0).then_inc(consts_ready, 1)
            pool.wait_ge(pool_step, 4)
            pool.affine_select(out=ident[:], in_=ident[:], compare_op=ALU.not_equal, fill=1.0, base=0,
                               pattern=[[-1, P]], channel_multiplier=1).then_inc(consts_ready, 1)
            pool.affine_select(out=ident_bf[:], in_=ident_bf[:], compare_op=ALU.not_equal, fill=1.0, base=0,
                               pattern=[[-1, P]], channel_multiplier=1).then_inc(consts_ready, 1)
            pool.affine_select(out=mask[:], in_=mask[:], compare_op=ALU.is_ge, fill=MASKED, base=0,
                               pattern=[[-1, P]], channel_multiplier=1).then_inc(consts_ready, 1)
            pool.affine_select(out=in_head[:], in_=in_head[:], compare_op=ALU.is_ge, fill=0.0, base=0,
                               pattern=[[-HD, P // HD]], channel_multiplier=1).then_inc(pool_step, 1)
            pool.wait_ge(pool_step, 5)
            pool.affine_select(out=in_head[:], in_=in_head[:], compare_op=ALU.is_ge, fill=0.0, base=HD - 1,
                               pattern=[[HD, P // HD]], channel_multiplier=-1).then_inc(consts_ready, 1)
            pool.wait_ge(consts_ready, NCONSTS)

            def inverse_std(n):
                pool.wait_ge(stats_ready, n + 1)
                pool.tensor_tensor(rstd[:], var_eps[:], minus_half[:], ALU.pow).then_inc(rstd_ready, 1)

            def step(k, s):
                if isinstance(s, int) and s >= STEPS:
                    return
                b = k % SPLITS
                pool.wait_ge(rows_high, s + 1)
                pool.tensor_tensor(rows_split[:, b, :, 1, :], rows_ring[:, k * STEP:(k + 1) * STEP, :],
                                   rows_split[:, b, :, 0, :].bitcast(F32), ALU.subtract).then_inc(rows_ready, 1)

            inverse_std(0)
            pipeline(pool, step)
            inverse_std(1)
            pool.wait_ge(x1_ready, 1)
            pool.wait_ge(weights_landed, 16 * len(weights))
            pool.tensor_tensor(x1_bias[:], x1[:], bproj_sb[:], ALU.add).then_inc(x1_bias_ready, 1)
            inverse_std(2)
            pool.wait_ge(x2_ready, 1)
            pool.tensor_tensor(x2_bias[:], x2[:], bffn_sb[:], ALU.add).then_inc(x2_bias_ready, 1)

        @block.tensor
        def _(pe):
            def turn_normed(n):
                pe.wait_ge(normed_ready, n + 1)
                for c in range(DC):
                    last = pe.transpose(turn[:, c * P:(c + 1) * P], normed[:, c * P:(c + 1) * P], ident[:])
                last.then_inc(turned, 1)

            def step(k, s):
                static = isinstance(s, int)
                if not static or s < STEPS:
                    if k % (CHUNK // STEP) == 0:
                        slot = k * STEP // CHUNK
                        pe.wait_ge(cols_landed[slot], 16 * (s // UNROLL + 1) if static
                                   else 2 * s + (16 - 2 * k))
                    if not static or s >= 2:
                        pe.wait_ge(exps_ready, s - 1)
                    for t in range(STEP):
                        for c in range(DC):
                            last = pe.matmul(scores[k % 2][:, t * P:(t + 1) * P],
                                             cols_ring[:, k * STEP + t, c, :], query_t[:, c, :],
                                             start=(c == 0), stop=(c == DC - 1))
                    last.then_inc(scores_ready, 1)
                if not static or s >= LAG:
                    b = k - LAG
                    pe.wait_ge(probs_ready, s - LAG + 1)
                    pe.wait_ge(rows_ready, s - LAG + 1)
                    for t in range(STEP):
                        pe.matmul(weighted[:], probs[:, b % SPLITS, t, 0, :],
                                  rows_split[:, b % SPLITS, t].rearrange("p i d -> p (i d)"),
                                  start=False, stop=False, skip_group_check=True)
                        last = pe.matmul(weighted[:, 0:D], probs[:, b % SPLITS, t, 1, :],
                                         rows_split[:, b % SPLITS, t, 0, :], start=False,
                                         stop=(static and s == STEPS + LAG - 1 and t == STEP - 1),
                                         skip_group_check=True)
                    last.then_inc(summed, 1)

            def keep_warm(count, into=turn[:]):
                for _ in range(count):
                    pe.matmul(into, warm[:, 0:P], warm[:, 0:into.shape[-1]], start=True, stop=True)

            def mask_scores(j):
                pe.matmul(head_scores[j][:], ident_bf[:], mask[:].unsqueeze(1).to_broadcast([P, HM, P]),
                          start=True, stop=False, skip_group_check=True)

            pe.wait_ge(warm_ready, 1)
            keep_warm(WARM_START)
            pe.wait_ge(consts_ready, NCONSTS)
            mask_scores(2)
            mask_scores(3)
            keep_warm(WARM_X)
            turn_normed(0)
            pe.matmul(weighted[:, 0:D], ident[:], x0[:], start=True, stop=False, skip_group_check=True)
            pe.matmul(weighted[:, D:2 * D], zeros[:], x0[:], start=False, stop=False, skip_group_check=True)
            pe.wait_ge(turn_copied, 1)
            pipeline(pe, step)

            pe.wait_ge(exps_ready, STEPS)
            mask_scores(0)
            mask_scores(1)
            pe.wait_ge(weights_landed, 16 * len(weights))
            pe.wait_ge(x1_ready, 1)
            pe.matmul(v_ps[:, 0:D], ones[:], bv_sb[:], start=True, stop=False, skip_group_check=True)
            keep_warm(WARM_NORM1)
            turn_normed(1)
            pe.wait_ge(turn_copied, 2)
            for n in range(2 * DC):
                ps = q_ps[:, n * P:(n + 1) * P] if n < DC else k_ps[n - DC][:, 0:P]
                for c in range(DC):
                    last = pe.matmul(ps, wqk_sb[:, c, n, :], normed_t[:, c, :], start=(c == 0), stop=(c == DC - 1))
                if n == DC - 1:
                    last.then_inc(q_ready, 1)
                elif n >= DC:
                    last.then_inc(k_ready, 1)
            for c in range(DC):
                last = pe.matmul(v_ps[:, 0:D], normed_t[:, c, :], wv_sb[:, c, :], start=False,
                                 stop=(c == DC - 1), skip_group_check=True)
            last.then_inc(v_ready, 1)
            pe.wait_ge(q_copied, 1)
            pe.wait_ge(k_copied, 1)
            pe.wait_ge(v_copied, 1)
            for j in range(GROUPS):
                rows = slice(32 * j, 32 * j + 32)
                for m in range(HM):
                    last = pe.matmul(head_scores[j][:, m * P:(m + 1) * P], q_t[rows, m // 2, :],
                                     k_t[rows, m // 2, m % 2, :], start=False, stop=True, skip_group_check=True)
                last.then_inc(head_scores_ready, 1)

            def weigh_values(j):
                pe.wait_ge(exp_t_copied[j], 1)
                for m in range(HM):
                    h = head_of(j, m)
                    last = pe.matmul(y_ps[:, h * HA:(h + 1) * HA], head_exp_t[:, j, m, :], v_ones[:, h, :],
                                     start=True, stop=True, skip_group_check=True)
                last.then_inc(y_summed, 1)

            for j in range(GROUPS):
                pe.wait_ge(head_exp_ready, j + 1)
                for m in range(HM):
                    last = pe.transpose(exp_t_ps[j][:, m * P:(m + 1) * P], head_exp[:, j, m, :], ident[:])
                last.then_inc(exp_turned, 1)
                keep_warm(WARM_HEADS, y_ps[:, NHEAD * HA:])
                if j >= 1:
                    weigh_values(j - 1)
                    if j < GROUPS - 1:
                        keep_warm(WARM_HEADS, y_ps[:, NHEAD * HA:])
            weigh_values(GROUPS - 1)
            keep_warm(WARM_Y)
            pe.wait_ge(y_ready, 1)
            for c in range(DC):
                last = pe.transpose(turn[:, c * P:(c + 1) * P],
                                    y[:].rearrange("p h d -> p (h d)")[:, c * P:(c + 1) * P], ident[:])
            last.then_inc(y_turned, 1)
            pe.wait_ge(y_t_copied, 1)
            for c in range(DC):
                last = pe.matmul(proj_ps[:, 0:D], y_t[:, c, :], wproj_sb[:, c, :], start=(c == 0),
                                 stop=(c == DC - 1))
            last.then_inc(proj_ready, 1)
            keep_warm(WARM_NORM2)
            turn_normed(2)
            pe.wait_ge(turn_copied, 3)
            for c in range(DC):
                last = pe.matmul(low_ps[0:R, 0:P], vr_sb[:, c, :], normed_t[:, c, :], start=(c == 0),
                                 stop=(c == DC - 1))
            last.then_inc(low_ready, 1)
            for c in range(DC):
                pe.matmul(ffn_ps[:, 0:D], normed_t[:, c, :], wffn_sb[:, c, :], start=(c == 0), stop=False)
            pe.wait_ge(low_copied, 1)
            pe.matmul(ffn_ps[:, 0:D], low_t[:], ct_sb[:], start=False, stop=True).then_inc(ffn_ready, 1)

        @block.scalar
        def _(act):
            def exp_step(k, s):
                static = isinstance(s, int)
                if static and s >= STEPS:
                    return
                if k % (CHUNK // STEP) == 0:
                    slot = k * STEP // CHUNK
                    act.wait_ge(rows_landed[slot], 16 * (s // UNROLL + 1) if static else 2 * s + (16 - 2 * k))
                if not static or s >= SPLITS:
                    act.wait_ge(summed, s - (SPLITS - 1))
                act.copy(rows_split[:, k % SPLITS, :, 0, :], rows_ring[:, k * STEP:(k + 1) * STEP, :])\
                   .then_inc(rows_high, 1)
                b = k % 2
                act.wait_ge(max_ready, s + 1)
                if not static or s >= 2:
                    act.wait_ge(probs_ready, s - 1)
                for t in range(STEP):
                    last = act.activation(exps[:, b, t, :], scores[b][:, t * P:(t + 1) * P], ACT.Exp,
                                          bias=neg_max[:, b, t:t + 1], accum_out=sums[:, b, t:t + 1])
                last.then_inc(exps_ready, 1)

            pipeline(act, exp_step)

            act.wait_ge(weights_landed, 16 * len(weights))
            act.wait_ge(q_ready, 1)
            for c in range(DC):
                last = act.activation(q_t[:, c, :], q_ps[:, c * P:(c + 1) * P], ACT.Identity, bias=bqk_sb[:, c:c + 1])
            last.then_inc(q_copied, 1)
            act.wait_ge(v_ready, 1)
            act.copy(v_ones[:, :, 0:HD], v_ps[:, 0:D].rearrange("p (h d) -> p h d", h=NHEAD)).then_inc(v_copied, 1)

            def copy_exp_t(j):
                act.wait_ge(exp_turned, j + 1)
                act.copy(head_exp_t[:, j].rearrange("p m q -> p (m q)"), exp_t_ps[j][:])\
                   .then_inc(exp_t_copied[j], 1)

            for j in range(GROUPS):
                if j % 2 == 0:
                    act.wait_ge(head_max_ready, j // 2 + 1)
                    for m in range(HM):
                        last = act.activation(head_exp[:, j, m, :], head_scores[j][:, m * P:(m + 1) * P], ACT.Exp,
                                              bias=head_max[:, j, m:m + 1], scale=SCALE)
                    last.then_inc(head_exp_ready, 1)
                else:
                    act.wait_ge(shifted_ready, j // 2 + 1)
                    act.activation(head_exp[:, j], shifted[:, j], ACT.Exp, scale=SCALE).then_inc(head_exp_ready, 1)
                if j == 2:
                    copy_exp_t(1)
            copy_exp_t(3)
            act.wait_ge(low_ready, 1)
            act.copy(low_t[:], low_ps[0:R, 0:P]).then_inc(low_copied, 1)

        @block.vector
        def _(dve):
            link_count = [0]

            def link(ins):
                link_count[0] += 1
                ins.then_inc(dve_step, 1)
                dve.wait_ge(dve_step, link_count[0])

            def layer_norm(n, src):
                link(dve.bn_stats(bn[:], src[:]))
                link(dve.bn_aggr(mean_var[:], bn[:]))
                dve.tensor_scalar(var_eps[:], mean_var[:, 1:2], EPS, None, ALU.add).then_inc(stats_ready, 1)
                if n == 2:
                    dve.tensor_scalar(normed[:], src[:], mean_var[:, 0:1], None, ALU.subtract).then_inc(normed_ready, 1)
                    return
                dve.wait_ge(rstd_ready, n + 1)
                dve.tensor_scalar(normed[:], src[:], mean_var[:, 0:1], rstd[:, 0:1], ALU.subtract, ALU.mult)\
                   .then_inc(normed_ready, 1)

            def copy_turn(n, dst):
                dve.wait_ge(turned, n + 1)
                dve.tensor_copy(dst[:].rearrange("p c t -> p (c t)"), turn[:, 0:D]).then_inc(turn_copied, 1)

            dve.memset(warm[:], 0.0).then_inc(warm_ready, 1)
            dve.wait_ge(x_landed, 16)
            layer_norm(0, x0)
            copy_turn(0, query_t)
            links_before = link_count[0]

            def step(k, s):
                static = isinstance(s, int)
                normalizes = (not static or s >= 1) and not (static and s > STEPS)
                if normalizes:
                    b, pb = (k - 1) % 2, (k - 1) % SPLITS
                    dve.wait_ge(exps_ready, s)
                    dve.reciprocal(inv_sums[:, b, :], sums[:, b, :]).then_inc(dve_step, 1)
                if not static or s < STEPS:
                    dve.wait_ge(scores_ready, s + 1)
                    dve.tensor_reduce(neg_max[:, k % 2, :],
                                      scores[k % 2][:, 0:STEP * P].rearrange("p (t q) -> p t q", q=P),
                                      AX_X, ALU.max, negate=True).then_inc(max_ready, 1)
                if normalizes:
                    if not static or s > SPLITS:
                        dve.wait_ge(summed, s - SPLITS)
                    dve.wait_ge(dve_step, s + links_before)
                    for t in range(STEP):
                        dve.tensor_scalar(probs[:, pb, t, 0, :], exps[:, b, t, :], inv_sums[:, b, t:t + 1],
                                          None, ALU.mult).then_inc(probs_high, 1)
                    for t in range(STEP):
                        dve.wait_ge(probs_high, STEP * s - (STEP - 1 - t))
                        last = dve.scalar_tensor_tensor(probs[:, pb, t, 1, :], exps[:, b, t, :],
                                                        inv_sums[:, b, t:t + 1], probs[:, pb, t, 0, :].bitcast(F32),
                                                        ALU.mult, ALU.subtract)
                    last.then_inc(probs_ready, 1)

            pipeline(dve, step)
            link_count[0] += STEPS

            dve.wait_ge(consts_ready, NCONSTS)
            dve.tensor_reduce(parity[:], in_head[:].rearrange("p (h e) -> p e h", e=2), AX_X, ALU.add)\
               .then_inc(parity_ready, 1)
            dve.wait_ge(weights_landed, 16 * len(weights))
            dve.wait_ge(summed, STEPS)
            link(dve.tensor_copy(x0[:], weighted[:, D:2 * D]))
            dve.tensor_tensor(x1[:], weighted[:, 0:D], x0[:], ALU.add).then_inc(x1_ready, 1)
            dve.wait_ge(x1_ready, 1)
            layer_norm(1, x1)
            copy_turn(1, normed_t)
            dve.wait_ge(parity_ready, 1)
            for c in range(DC):
                dve.wait_ge(k_ready, c + 1)
                for e in range(2):
                    last = dve.tensor_scalar(k_t[:, c, e, :], k_ps[c][:, 0:P], bqk_sb[:, DC + c:DC + c + 1],
                                             parity[:, e:e + 1], ALU.add, ALU.mult)
            last.then_inc(k_copied, 1)

            def copy_exp_t(j):
                dve.wait_ge(exp_turned, j + 1)
                dve.tensor_copy(head_exp_t[:, j].rearrange("p m q -> p (m q)"), exp_t_ps[j][:])\
                   .then_inc(exp_t_copied[j], 1)

            for j in range(GROUPS):
                dve.wait_ge(head_scores_ready, j + 1)
                s_view = head_scores[j][:].rearrange("p (m k) -> p m k", k=P)
                if j % 2 == 0:
                    link(dve.tensor_reduce(head_max[:, j, :], s_view, AX_X, ALU.max, negate=True))
                    dve.tensor_scalar(head_max[:, j, :], head_max[:, j, :], SCALE, None, ALU.mult)\
                       .then_inc(head_max_ready, 1)
                else:
                    link(dve.tensor_reduce(head_max[:, j, :], s_view, AX_X, ALU.max))
                    dve.tensor_tensor(shifted[:, j], s_view,
                                      head_max[:, j, :].unsqueeze(2).to_broadcast([P, HM, P]),
                                      ALU.subtract).then_inc(shifted_ready, 1)
                    if j == 1:
                        copy_exp_t(0)
            copy_exp_t(2)
            dve.wait_ge(y_summed, GROUPS)
            y_view = y_ps[:, 0:NHEAD * HA].rearrange("p (h a) -> p h a", a=HA)
            link(dve.reciprocal(head_inv[:], y_view[:, :, HD]))
            dve.tensor_tensor(y[:], y_view[:, :, 0:HD], head_inv[:].unsqueeze(2).to_broadcast([P, NHEAD, HD]),
                              ALU.mult).then_inc(y_ready, 1)
            dve.wait_ge(y_turned, 1)
            dve.tensor_copy(y_t[:].rearrange("p c t -> p (c t)"), turn[:, 0:D]).then_inc(y_t_copied, 1)
            dve.wait_ge(proj_ready, 1)
            dve.wait_ge(x1_bias_ready, 1)
            dve.tensor_tensor(x2[:], proj_ps[:, 0:D], x1_bias[:], ALU.add).then_inc(x2_ready, 1)
            dve.wait_ge(x2_ready, 1)
            layer_norm(2, x2)
            copy_turn(2, normed_t)
            dve.wait_ge(ffn_ready, 1)
            dve.wait_ge(x2_bias_ready, 1)
            dve.wait_ge(rstd_ready, 3)
            dve.scalar_tensor_tensor(x3[:], ffn_ps[:, 0:D], rstd[:, 0:1], x2_bias[:], ALU.mult, ALU.add)\
               .then_inc(x3_ready, 1)


def kernel(**inputs):
    import numpy as np
    import concourse.bacc as bacc
    from concourse import mybir as mb
    from concourse.bass_utils import run_bass_kernel_spmd

    x = np.asarray(inputs["x"])[0]
    context = np.asarray(inputs["ctx_1024"])[0]
    w_attn = np.asarray(inputs["L0_attn_w_attn"])
    b_attn = np.asarray(inputs["L0_attn_b_attn"])
    D = x.shape[1]
    DC, TILES = D // P, context.shape[0] // P

    def chunked(w):
        return np.ascontiguousarray(w.reshape(-1, P, w.shape[-1]).transpose(1, 0, 2))

    tiles = context.reshape(TILES, P, DC, P)
    arrays = {
        "x": x,
        "ctx_rows": tiles.transpose(1, 0, 2, 3).reshape(P, TILES * D),
        "ctx_cols": tiles.transpose(3, 0, 2, 1).reshape(P, TILES * D),
        "w_qk": chunked(w_attn[:, 0:2 * D]).reshape(P, DC, 2 * DC, P),
        "b_qk": b_attn[0:2 * D].reshape(2 * DC, P).T,
        "w_v": chunked(w_attn[:, 2 * D:]),
        "b_v": b_attn[None, 2 * D:],
        "w_proj": chunked(np.asarray(inputs["L0_attn_w_proj"])),
        "b_proj": np.asarray(inputs["L0_attn_b_proj"])[None],
        "w_ffn": chunked(np.asarray(inputs["L0_ffn_W"]).T),
        "b_ffn": np.asarray(inputs["L0_ffn_b"])[None],
        "v_r": chunked(np.asarray(inputs["L0_ffn_V_r"])),
        "c_t": np.asarray(inputs["L0_ffn_C"]).T,
    }
    arrays = {f"{name}_dram": np.ascontiguousarray(a) for name, a in arrays.items()}
    nc = bacc.Bacc("TRN2", target_bir_lowering=False, num_devices=1)
    args = [nc.dram_tensor(name, a.shape, mb.dt.from_np(a.dtype), kind="ExternalInput").ap()
            for name, a in arrays.items()]
    out = nc.dram_tensor("out_dram", x.shape, mb.dt.from_np(x.dtype), kind="ExternalOutput").ap()
    perceiver_kernel(nc, *args, out)
    result = run_bass_kernel_spmd(nc, [arrays], core_ids=[0])
    return result.results[0]["out_dram"][None]
```
